# Optimizing a Trainium2 kernel written in Bass

```python
import numpy as np
import jax
import jax.numpy as jnp

def _softmax(x, axis=-1):
    return jax.nn.softmax(x, axis=axis)

def _gelu(x):
    return jax.nn.gelu(x, approximate=True)

def _silu(x):
    return jax.nn.silu(x)

def _sigmoid(x):
    return jax.nn.sigmoid(x)

def _layernorm(x, axis=-1, eps=1e-05):
    m = jnp.mean(x, axis=axis, keepdims=True)
    v = jnp.var(x, axis=axis, keepdims=True)
    return (x - m) / jnp.sqrt(v + eps)

def _scatter_add(tgt, idx, src, axis=0):
    return tgt.at[idx].add(src)

def _segment_sum(src, seg, n):
    return jax.ops.segment_sum(src, seg, n)
kernel_name = 'mk_rec_standalone_d1_rec_r8_9e02f9'

def setup_inputs(seed: int=0):
    np.random.seed(seed)
    _w = jnp.asarray

    def _rec_inputs():
        import jax
        import jax.numpy as jnp
        _rk = jax.random.key(seed)
        r_input_data = jax.random.uniform(jax.random.fold_in(_rk, 1), (512, 12500), jnp.float32, 0.0, 1)
        return r_input_data
    r_input_data = _rec_inputs()

    def _L0_rec_setup():
        import jax, jax.numpy as jnp
        import numpy as np
        B, N_DIMS, EMBED_DIM = (1024, 12500, 16)
        H1, H2 = (128, 64)

        def _xavier(key, shape):
            fan_in, fan_out = (shape[-1], shape[-2] if len(shape) > 1 else shape[-1])
            lim = jnp.sqrt(6.0 / (fan_in + fan_out)).astype(jnp.float32)
            return jax.random.uniform(key, shape, jnp.float32, -lim, lim)
        key = jax.random.key(seed)
        ks = jax.random.split(key, 9)
        input_data = jax.random.uniform(ks[0], (B, N_DIMS), jnp.float32)
        W_lin = _xavier(ks[1], (1, N_DIMS))
        b_lin = jnp.zeros((1,), jnp.float32)
        factors = _xavier(ks[2], (N_DIMS, EMBED_DIM))
        W1 = _xavier(ks[3], (H1, EMBED_DIM))
        b1 = jnp.zeros((H1,), jnp.float32)
        W2 = _xavier(ks[4], (H2, H1))
        b2 = jnp.zeros((H2,), jnp.float32)
        W3 = _xavier(ks[5], (1, H2))
        b3 = jnp.zeros((1,), jnp.float32)
        return {'input_data': input_data, 'W_lin': W_lin, 'b_lin': b_lin, 'factors': factors, 'W1': W1, 'b1': b1, 'W2': W2, 'b2': b2, 'W3': W3, 'b3': b3}
    _L0_rec_all = _L0_rec_setup()
    _L0_rec_in = {k: v for k, v in _L0_rec_all.items() if k in ('W_lin', 'b_lin', 'factors', 'W1', 'b1', 'W2', 'b2', 'W3', 'b3')}
    del _L0_rec_all
    return {'r_input_data': r_input_data, 'L0_rec_W_lin': _L0_rec_in['W_lin'], 'L0_rec_b_lin': _L0_rec_in['b_lin'], 'L0_rec_factors': _L0_rec_in['factors'], 'L0_rec_W1': _L0_rec_in['W1'], 'L0_rec_b1': _L0_rec_in['b1'], 'L0_rec_W2': _L0_rec_in['W2'], 'L0_rec_b2': _L0_rec_in['b2'], 'L0_rec_W3': _L0_rec_in['W3'], 'L0_rec_b3': _L0_rec_in['b3']}

def reference(r_input_data, L0_rec_W_lin, L0_rec_b_lin, L0_rec_factors, L0_rec_W1, L0_rec_b1, L0_rec_W2, L0_rec_b2, L0_rec_W3, L0_rec_b3):
    import jax
    import jax.numpy as jnp

    def _L0_rec_ref(input_data, W_lin, b_lin, factors, W1, b1, W2, b2, W3, b3):
        import jax, jax.numpy as jnp
        import numpy as np
        B, N_DIMS, EMBED_DIM = (1024, 12500, 16)
        H1, H2 = (128, 64)

        def _xavier(key, shape):
            fan_in, fan_out = (shape[-1], shape[-2] if len(shape) > 1 else shape[-1])
            lim = jnp.sqrt(6.0 / (fan_in + fan_out)).astype(jnp.float32)
            return jax.random.uniform(key, shape, jnp.float32, -lim, lim)
        x_reg = input_data @ W_lin.T + b_lin
        emb = input_data @ factors
        sum_squared = jnp.square(emb.sum(axis=1))
        squared_sum = (jnp.square(input_data) @ jnp.square(factors)).sum(axis=1)
        h = jax.nn.relu(emb @ W1.T + b1)
        h = jax.nn.relu(h @ W2.T + b2)
        dnn_out = h @ W3.T + b3
        x = x_reg + 0.5 * (sum_squared - squared_sum)[:, None] + dnn_out
        x = 0.5 + jax.nn.sigmoid(x) * 5.0
        return x.squeeze()
    y = _L0_rec_ref(r_input_data, L0_rec_W_lin, L0_rec_b_lin, L0_rec_factors, L0_rec_W1, L0_rec_b1, L0_rec_W2, L0_rec_b2, L0_rec_W3, L0_rec_b3)
    return y

_drawn_inputs = setup_inputs


def setup_inputs(seed=0):
    import zlib

    import numpy as np

    out = dict(_drawn_inputs(seed))
    spreads = {'L0_rec_b1': (0.0, 0.8), 'L0_rec_b2': (0.0, 2.0)}
    factors = {'L0_rec_W2': 4.205,
     'r_input_data': 3.761,
     'L0_rec_W_lin': 8.0,
     'L0_rec_factors': 4.932,
     'L0_rec_W1': 7.117}
    for name, (base, spread) in spreads.items():
        noise = np.random.default_rng([zlib.crc32(name.encode()), seed]).standard_normal(out[name].shape)
        drawn = base * np.exp(spread * noise) if base else spread * noise
        out[name] = jnp.asarray(drawn.astype(out[name].dtype))
    for name, factor in factors.items():
        out[name] = (out[name] * factor).astype(out[name].dtype)
    return out
```

```python
from contextlib import ExitStack

import concourse.bass as bass
from concourse import mybir

F32 = mybir.dt.float32
BF16 = mybir.dt.bfloat16
ALU = mybir.AluOpType
ACT = mybir.ActivationFunctionType
AX_X = mybir.AxisListType.X

P = 128
B = 512
D = 12500
E = 16
H1, H2 = 128, 64
QUAD = 32
TILES = P // QUAD

CHUNKS = -(-D // P)
WCOL = E + 1
CW = B + WCOL
GROUP = TILES
RING = 4
LAPS = CHUNKS // (GROUP * RING)
GROUPS = LAPS * RING
LAST = CHUNKS - GROUPS * GROUP
SQ_RING = 2
ACT_CHUNKS = 2

C_W1, C_W2, C_W3 = 0, H1, H1 + H2
C_B1, C_B2, C_BLIN, C_B3 = C_W3 + 1, C_W3 + 2, C_W3 + 3, C_W3 + 4
C_LIN, C_FAC, C_SQ = C_W3 + 5, C_W3 + 6, C_W3 + 7
C_ALL = C_W3 + 8


def build(nc, x_groups, x_last, head, out):
    with ExitStack() as ctx:
        def sb(name, shape, dt=F32):
            return ctx.enter_context(nc.sbuf_tensor(name, shape, dt))

        def psum(name, shape):
            return ctx.enter_context(nc.psum_tensor(name, shape, F32))

        def sem(name):
            return ctx.enter_context(nc.semaphore(name))

        xw = sb("xw", [P, RING + 1, GROUP, CW])
        sq = sb("sq", [P, SQ_RING, GROUP, B])
        fsq = sb("fsq", [P, GROUP, E])
        g = sb("g", [P, SQ_RING, GROUP])
        hp = sb("hp", [P, C_ALL])
        bias = sb("bias", [P, 1])
        zeros = sb("zeros", [P, B], BF16)
        emb_sb = sb("emb_sb", [P, B])
        sqs_sb = sb("sqs_sb", [P, B])
        h1_sb = sb("h1_sb", [P, B])
        h2_sb = sb("h2_sb", [H2, B])
        s2 = sb("s2", [P, TILES])
        z = sb("z", [P, TILES])
        sig = sb("sig", [P, TILES])
        y = sb("y", [P, TILES])

        emb = psum("emb", [P, B])
        sqs = psum("sqs", [P, B])
        h1 = psum("h1", [P, B])
        h2 = psum("h2", [P, B])
        fin = psum("fin", [P, B])

        loaded = [sem(f"loaded{r}") for r in range(RING + 1)]
        head_loaded = sem("head_loaded")
        groups_used = sem("groups_used")
        act_squared = sem("act_squared")
        dve_squared = sem("dve_squared")
        fsq_done = sem("fsq_done")
        g_done = sem("g_done")
        emb_done = sem("emb_done")
        sqs_done = sem("sqs_done")
        emb_copied = sem("emb_copied")
        sqs_copied = sem("sqs_copied")
        h1_done = sem("h1_done")
        h1_relu = sem("h1_relu")
        h2_done = sem("h2_done")
        h2_relu = sem("h2_relu")
        bias_done = sem("bias_done")
        sums_done = sem("sums_done")
        s2_done = sem("s2_done")
        fin_done = sem("fin_done")
        z_done = sem("z_done")
        sig_done = sem("sig_done")
        y_done = sem("y_done")
        stored = sem("stored")

        block = ctx.enter_context(nc.Block())

        @block.sync
        def _(sp):
            for r in range(RING):
                sp.dma_start(xw[:, r, :, :], x_groups[r]).then_inc(loaded[r], 16)
            sp.dma_start(hp[:, :], head).then_inc(head_loaded, 16)
            with sp.Fori(1, LAPS) as lap:
                for r in range(RING):
                    sp.wait_ge(groups_used, SQ_RING + (lap - 1) * RING + r + 1)
                    sp.dma_start(xw[:, r, :, :], x_groups[bass.ds(lap * RING + r, 1)]).then_inc(loaded[r], 16)
            sp.dma_start(xw[:, RING, 0:LAST, :], x_last).then_inc(loaded[RING], 16)
            sp.wait_ge(y_done, 1)
            sp.dma_start(out.rearrange("(p j) -> p j", j=TILES), y[:, :]).then_inc(stored, 16)
            sp.wait_ge(stored, 16)

        @block.gpsimd
        def _(pool):
            nc.gpsimd.memset(zeros[:, :], 0.0).then_inc(groups_used, SQ_RING)

        @block.scalar
        def _(act):
            def square(r, s, chunks):
                return nc.scalar.activation(sq[:, s, 0:chunks, :], xw[:, r, 0:chunks, 0:B], ACT.Square)

            with act.Fori(0, LAPS) as lap:
                for r in range(RING):
                    n = lap * RING + r
                    act.wait_ge(loaded[r], (lap + 1) * 16)
                    act.wait_ge(groups_used, n + 1)
                    square(r, r % SQ_RING, ACT_CHUNKS).then_inc(act_squared, 1)
            act.wait_ge(loaded[RING], 16)
            act.wait_ge(groups_used, GROUPS + 1)
            square(RING, GROUPS % SQ_RING, LAST // 2).then_inc(act_squared, 1)

            act.wait_ge(emb_done, 1)
            nc.scalar.copy(emb_sb[:, :], emb[:, :]).then_inc(emb_copied, 1)
            act.wait_ge(head_loaded, 16)
            act.wait_ge(h1_done, 1)
            nc.scalar.activation(h1_sb[:, :], h1[:, :], ACT.Relu, bias=hp[:, C_B1:C_B1 + 1]).then_inc(h1_relu, 1)
            act.wait_ge(sums_done, 1)
            nc.scalar.activation(s2[:, :], fin[:, TILES:2 * TILES], ACT.Square).then_inc(s2_done, 1)
            act.wait_ge(z_done, 1)
            act.wait_ge(bias_done, 1)
            nc.scalar.activation(sig[:, :], z[:, :], ACT.Sigmoid, bias=bias[:, :]).then_inc(sig_done, 1)

        @block.vector
        def _(dve):
            def factors_squared(r, chunks):
                f = xw[:, r, 0:chunks, B:B + E]
                return nc.vector.scalar_tensor_tensor(out=fsq[:, 0:chunks, :], in0=f, scalar=-0.5, in1=f,
                                                      op0=ALU.mult, op1=ALU.mult)

            def square(r, s, c0, c1):
                x = xw[:, r, c0:c1, 0:B]
                return nc.vector.tensor_tensor(sq[:, s, c0:c1, :], x, x, ALU.mult)

            def factor_sum(s, chunks):
                return nc.vector.tensor_reduce(g[:, s, 0:chunks], fsq[:, 0:chunks, :], AX_X, ALU.add)

            with dve.Fori(0, LAPS) as lap:
                for r in range(RING):
                    n = lap * RING + r
                    dve.wait_ge(loaded[r], (lap + 1) * 16)
                    dve.wait_ge(groups_used, n + 1)
                    dve.wait_ge(g_done, n)
                    factors_squared(r, GROUP).then_inc(fsq_done, 1)
                    square(r, r % SQ_RING, ACT_CHUNKS, GROUP).then_inc(dve_squared, 1)
                    dve.wait_ge(fsq_done, n + 1)
                    factor_sum(r % SQ_RING, GROUP).then_inc(g_done, 1)
            dve.wait_ge(loaded[RING], 16)
            dve.wait_ge(groups_used, GROUPS + 1)
            dve.wait_ge(g_done, GROUPS)
            factors_squared(RING, LAST).then_inc(fsq_done, 1)
            square(RING, GROUPS % SQ_RING, LAST // 2, LAST).then_inc(dve_squared, 1)
            dve.wait_ge(fsq_done, GROUPS + 1)
            factor_sum(GROUPS % SQ_RING, LAST).then_inc(g_done, 1)

            dve.wait_ge(head_loaded, 16)
            nc.vector.tensor_tensor(bias[:, :], hp[:, C_BLIN:C_BLIN + 1], hp[:, C_B3:C_B3 + 1],
                                    ALU.add).then_inc(bias_done, 1)
            dve.wait_ge(sqs_done, 1)
            nc.vector.tensor_copy(sqs_sb[:, :], sqs[:, :]).then_inc(sqs_copied, 1)
            dve.wait_ge(h2_done, 1)
            nc.vector.tensor_scalar(h2_sb[:, :], h2[0:H2, :], hp[0:H2, C_B2:C_B2 + 1], 0.0,
                                    ALU.add, ALU.max).then_inc(h2_relu, 1)
            dve.wait_ge(s2_done, 1)
            dve.wait_ge(fin_done, 1)
            nc.vector.scalar_tensor_tensor(out=z[:, :], in0=s2[:, :], scalar=0.5, in1=fin[:, 0:TILES],
                                           op0=ALU.mult, op1=ALU.add).then_inc(z_done, 1)
            dve.wait_ge(sig_done, 1)
            nc.vector.tensor_scalar(y[:, :], sig[:, :], 5.0, 0.5, ALU.mult, ALU.add).then_inc(y_done, 1)

        @block.tensor
        def _(pe):
            pe.wait_ge(groups_used, SQ_RING)
            for acc in (emb, sqs):
                for j in range(TILES):
                    nc.tensor.matmul(acc[QUAD * j:QUAD * (j + 1), :], zeros[:, 0:QUAD], zeros[:, :],
                                     start=True, stop=True)
            nc.tensor.matmul(fin[:, 0:2 * TILES], zeros[:, 0:P], zeros[:, 0:2 * TILES], start=True, stop=True)

            def products(r, chunks):
                for c in range(chunks):
                    last = nc.tensor.matmul(emb[QUAD * c:QUAD * c + WCOL, :], xw[:, r, c, B:CW], xw[:, r, c, 0:B],
                                            start=False, stop=True, skip_group_check=True)
                return last

            def square_products(s, chunks):
                for c in range(chunks):
                    last = nc.tensor.matmul(sqs[QUAD * c:QUAD * c + 1, :], g[:, s, c:c + 1], sq[:, s, c, :],
                                            start=False, stop=True, skip_group_check=True)
                return last

            with pe.Fori(0, LAPS) as lap:
                for r in range(RING):
                    n = lap * RING + r
                    pe.wait_ge(loaded[r], (lap + 1) * 16)
                    products(r, GROUP)
                    pe.wait_ge(act_squared, n + 1)
                    pe.wait_ge(dve_squared, n + 1)
                    pe.wait_ge(g_done, n + 1)
                    square_products(r % SQ_RING, GROUP).then_inc(groups_used, 1)
            pe.wait_ge(loaded[RING], 16)
            products(RING, LAST).then_inc(emb_done, 1)
            pe.wait_ge(act_squared, GROUPS + 1)
            pe.wait_ge(dve_squared, GROUPS + 1)
            pe.wait_ge(g_done, GROUPS + 1)
            square_products(GROUPS % SQ_RING, LAST).then_inc(sqs_done, 1)

            pe.wait_ge(head_loaded, 16)
            pe.wait_ge(emb_copied, 1)
            nc.tensor.matmul(h1[:, :], hp[:, C_W1:C_W1 + H1], emb_sb[:, :], start=True, stop=True).then_inc(h1_done, 1)
            for j in range(TILES):
                nc.tensor.matmul(fin[:, j:j + 1], emb_sb[:, j::TILES], hp[:, C_LIN:C_LIN + 1],
                                 start=False, stop=True, skip_group_check=True)
                last = nc.tensor.matmul(fin[:, TILES + j:TILES + j + 1], emb_sb[:, j::TILES], hp[:, C_FAC:C_FAC + 1],
                                        start=False, stop=True, skip_group_check=True)
            pe.wait_ge(sqs_copied, 1)
            for j in range(TILES):
                last = nc.tensor.matmul(fin[:, j:j + 1], sqs_sb[:, j::TILES], hp[:, C_SQ:C_SQ + 1],
                                        start=False, stop=True, skip_group_check=True)
            last.then_inc(sums_done, 1)
            pe.wait_ge(h1_relu, 1)
            nc.tensor.matmul(h2[0:H2, :], hp[:, C_W2:C_W2 + H2], h1_sb[:, :], start=True, stop=True).then_inc(h2_done, 1)
            pe.wait_ge(h2_relu, 1)
            pe.wait_ge(s2_done, 1)
            for j in range(TILES):
                last = nc.tensor.matmul(fin[:, j:j + 1], h2_sb[:, j::TILES], hp[0:H2, C_W3:C_W3 + 1],
                                        start=False, stop=True, skip_group_check=True)
            last.then_inc(fin_done, 1)


def kernel(r_input_data, L0_rec_W_lin, L0_rec_b_lin, L0_rec_factors, L0_rec_W1, L0_rec_b1,
           L0_rec_W2, L0_rec_b2, L0_rec_W3, L0_rec_b3):
    import numpy as np
    import concourse.bacc as bacc
    from concourse.bass_utils import run_bass_kernel_spmd

    rows = np.zeros((CHUNKS * P, CW), np.float32)
    rows[:D, 0:B] = np.asarray(r_input_data).T
    rows[:D, B:B + E] = np.asarray(L0_rec_factors)
    rows[:D, B + E] = np.asarray(L0_rec_W_lin)[0]
    looped = GROUPS * GROUP * P
    x_groups = np.ascontiguousarray(
        rows[:looped].reshape(GROUPS, GROUP, P, CW).transpose(0, 2, 1, 3))
    x_last = np.ascontiguousarray(rows[looped:].reshape(LAST, P, CW).transpose(1, 0, 2))

    head = np.zeros((P, C_ALL), np.float32)
    for j in range(TILES):
        q = QUAD * j
        head[q:q + E, C_W1:C_W1 + H1] = np.asarray(L0_rec_W1).T
        head[q + E, C_LIN] = 1
        head[q:q + E, C_FAC] = 1
        head[q, C_SQ] = 1
    head[:H1, C_W2:C_W2 + H2] = np.asarray(L0_rec_W2).T
    head[:H2, C_W3] = np.asarray(L0_rec_W3)[0]
    head[:H1, C_B1] = np.asarray(L0_rec_b1)
    head[:H2, C_B2] = np.asarray(L0_rec_b2)
    head[:, C_BLIN] = np.asarray(L0_rec_b_lin)[0]
    head[:, C_B3] = np.asarray(L0_rec_b3)[0]

    nc = bacc.Bacc("TRN2", target_bir_lowering=False, num_devices=1)
    arrays = {"x_groups": x_groups, "x_last": x_last, "head": head}
    args = [nc.dram_tensor(name, a.shape, F32, kind="ExternalInput").ap() for name, a in arrays.items()]
    args.append(nc.dram_tensor("out", (B,), F32, kind="ExternalOutput").ap())
    build(nc, *args)
    return run_bass_kernel_spmd(nc, [arrays], core_ids=[0]).results[0]["out"]
```

```python
from contextlib import ExitStack

import concourse.bass as bass
from concourse import mybir

F32 = mybir.dt.float32
BF16 = mybir.dt.bfloat16
ALU = mybir.AluOpType
ACT = mybir.ActivationFunctionType
AX_X = mybir.AxisListType.X

P = 128
B = 512
D = 12500
E = 16
H1, H2 = 128, 64
QUAD = 32
TILES = P // QUAD
HALF = B // 2
BLOCK = B // TILES

CHUNKS = -(-D // P)
LAST_ROWS = D - (CHUNKS - 1) * P
W = E + 1
GROUP = TILES
RING = 4
SLOTS = 2
LAPS = 5
GROUPS = LAPS * RING
LOOPED = GROUPS * GROUP
TAIL = (4, 4, 4, 2, 2, 1, 1)
TAIL_CHUNKS = CHUNKS - LOOPED
assert sum(TAIL) == TAIL_CHUNKS and TAIL[-1] == 1

C_W1 = 0
C_W2 = C_W1 + H1
C_W3 = C_W2 + H2
C_B1 = C_W3 + 2
C_B2 = C_B1 + 1
C_BLIN = C_B2 + 1
C_B3 = C_BLIN + 1
C_LIN = C_B3 + 1
C_FAC = C_LIN + 1
C_SQ = C_FAC + 1
C_HALF = C_SQ + 1
C_TAIL = C_HALF + TILES
C_ALL = C_TAIL + TAIL_CHUNKS * W


def build(nc, w_loop, x_loop, x_tail, x_end, params, out):
    with ExitStack() as ctx:
        def sb(name, shape, dt=F32):
            return ctx.enter_context(nc.sbuf_tensor(name, shape, dt))

        def psum(name, shape):
            return ctx.enter_context(nc.psum_tensor(name, shape, F32))

        def sem(name):
            return ctx.enter_context(nc.semaphore(name))

        x = sb("x", [P, RING, GROUP * B])
        sq = sb("sq", [P, SLOTS, GROUP * B])
        xt = sb("xt", [P, TAIL_CHUNKS * B])
        sqt = sb("sqt", [P, TAIL_CHUNKS * B])
        w_all = sb("w_all", [P, LOOPED, W])
        fsq = sb("fsq", [P, LOOPED, E])
        g_all = sb("g_all", [P, LOOPED])
        fsqt = sb("fsqt", [P, TAIL_CHUNKS, E])
        gt = sb("gt", [P, TAIL_CHUNKS])
        w = sb("w", [P, SLOTS, GROUP * W])
        g = sb("g", [P, SLOTS, GROUP])
        par = sb("par", [P, C_ALL])
        zeros = sb("zeros", [P, B], BF16)
        warm = sb("warm", [P, 1])
        emb_sb = sb("emb_sb", [P, B])
        sqs_sb = sb("sqs_sb", [P, B])
        h1_sb = sb("h1_sb", [P, B])
        h2_sb = sb("h2_sb", [P, HALF])
        bias = sb("bias", [P, 1])
        s2 = sb("s2", [P, BLOCK])
        sig = sb("sig", [P, BLOCK])
        y = sb("y", [P, BLOCK])

        emb = psum("emb", [P, B])
        sqs = psum("sqs", [P, B])
        h1 = [psum(f"h1_{q}", [P, B]) for q in range(TILES)]
        sums = psum("sums", [P, B])
        fin = psum("fin", [P, B])

        w_loaded = sem("w_loaded")
        loaded = [sem(f"loaded{r}") for r in range(RING)]
        tail_loaded = [sem(f"tail_loaded{t}") for t in range(len(TAIL))]
        par_loaded = sem("par_loaded")
        groups_used = sem("groups_used")
        w_ready = sem("w_ready")
        act_squared = sem("act_squared")
        dve_squared = sem("dve_squared")
        fsq_done = sem("fsq_done")
        g_done = sem("g_done")
        emb_done = sem("emb_done")
        sqs_done = sem("sqs_done")
        emb_copied = sem("emb_copied")
        sqs_copied = sem("sqs_copied")
        h1_done = sem("h1_done")
        h1_relu = [sem(f"h1_relu{q}") for q in range(TILES)]
        h2_done = sem("h2_done")
        h2_relu = sem("h2_relu")
        bias_done = sem("bias_done")
        sums_done = sem("sums_done")
        s2_done = sem("s2_done")
        fin_done = sem("fin_done")
        sig_done = sem("sig_done")
        y_done = sem("y_done")
        stored = sem("stored")

        tail = [(t, sum(TAIL[:t]), n, P if t < len(TAIL) - 1 else LAST_ROWS) for t, n in enumerate(TAIL)]

        def h1_of(q):
            return h1[q][:, 0:BLOCK], h1_sb[:, q * BLOCK:(q + 1) * BLOCK]

        def h2_of(q):
            rows = slice(q // 2 * H2, (q // 2 + 1) * H2)
            bank = (emb, h1[0])[q % 2]
            return bank[rows, 0:BLOCK], h2_sb[rows, q % 2 * BLOCK:(q % 2 + 1) * BLOCK]

        b1 = par[:, C_B1:C_B1 + 1]

        def b2(q):
            return par[q // 2 * H2:(q // 2 + 1) * H2, C_B2:C_B2 + 1]

        block = ctx.enter_context(nc.Block())

        @block.sync
        def _(sp):
            sp.dma_start(w_all[:, :, :], w_loop).then_inc(w_loaded, 16)
            for r in range(RING):
                sp.dma_start(x[:, r, :], x_loop[r]).then_inc(loaded[r], 16)
            sp.dma_start(par[:, :], params).then_inc(par_loaded, 16)
            with sp.Fori(1, LAPS) as lap:
                for r in range(RING):
                    sp.wait_ge(groups_used, SLOTS + (lap - 1) * RING + r + 1)
                    sp.dma_start(x[:, r, :], x_loop[bass.ds(lap * RING + r, 1)]).then_inc(loaded[r], 16)
            for t, c, n, rows in tail:
                src = x_end if t == len(TAIL) - 1 else x_tail[:, c * B:(c + n) * B]
                sp.dma_start(xt[0:rows, c * B:(c + n) * B], src).then_inc(tail_loaded[t], 16)
            sp.wait_ge(y_done, 1)
            sp.dma_start(out.rearrange("(q b) -> q b", b=BLOCK), y[::QUAD, :]).then_inc(stored, 16)
            sp.wait_ge(stored, 16)

        @block.gpsimd
        def _(pool):
            nc.gpsimd.memset(zeros[:, :], 0.0).then_inc(groups_used, SLOTS)
            pool.wait_ge(w_loaded, 16)
            pool.wait_ge(g_done, 1)
            with pool.Fori(0, LAPS) as lap:
                for r in range(RING):
                    n = lap * RING + r
                    pool.wait_ge(groups_used, n + 1)
                    nc.gpsimd.tensor_copy(w[:, r % SLOTS, :].rearrange("p (c k) -> p c k", k=W),
                                          w_all[:, bass.ds(n * GROUP, GROUP), :])
                    nc.gpsimd.tensor_copy(g[:, r % SLOTS, :],
                                          g_all[:, bass.ds(n * GROUP, GROUP)]).then_inc(w_ready, 1)

        @block.scalar
        def _(act):
            nc.scalar.activation(warm[:, :], nc.const_aps.tensor(0.0, (P, 1), F32), ACT.Sigmoid)

            with act.Fori(0, LAPS) as lap:
                for r in range(RING):
                    n = lap * RING + r
                    act.wait_ge(loaded[r], (lap + 1) * 16)
                    act.wait_ge(groups_used, n + 1)
                    nc.scalar.activation(sq[:, r % SLOTS, 0:GROUP * B // 2], x[:, r, 0:GROUP * B // 2],
                                         ACT.Square).then_inc(act_squared, 1)
            for t, c, n, rows in tail:
                act.wait_ge(tail_loaded[t], 16)
                half = slice(c * B, c * B + n * HALF)
                nc.scalar.activation(sqt[0:rows, half], xt[0:rows, half], ACT.Square).then_inc(act_squared, 1)

            act.wait_ge(emb_done, 1)
            for q in range(TILES):
                cols = slice(q * BLOCK, (q + 1) * BLOCK)
                nc.scalar.copy(emb_sb[:, cols], emb[:, cols]).then_inc(emb_copied, 1)
            act.wait_ge(sqs_done, 1)
            nc.scalar.copy(sqs_sb[:, 0:HALF], sqs[:, 0:HALF]).then_inc(sqs_copied, 1)
            act.wait_ge(par_loaded, 16)
            for q in range(1, TILES, 2):
                act.wait_ge(h1_done, q + 1)
                src, dst = h1_of(q)
                nc.scalar.activation(dst, src, ACT.Relu, bias=b1).then_inc(h1_relu[q], 1)
            act.wait_ge(sums_done, 1)
            nc.scalar.activation(s2[:, :], sums[:, 0:BLOCK], ACT.Square).then_inc(s2_done, 1)
            for q in range(1, TILES, 2):
                act.wait_ge(h2_done, q + 1)
                src, dst = h2_of(q)
                nc.scalar.activation(dst, src, ACT.Relu, bias=b2(q)).then_inc(h2_relu, 1)
            act.wait_ge(bias_done, 1)
            act.wait_ge(fin_done, 1)
            nc.scalar.activation(sig[:, :], fin[:, 0:BLOCK], ACT.Sigmoid, bias=bias[:, :]).then_inc(sig_done, 1)

        @block.vector
        def _(dve):
            def square(dst, src, done):
                nc.vector.tensor_tensor(dst, src, src, ALU.mult).then_inc(done, 1)

            def factor_sums(fsq_, g_, f, count):
                nc.vector.scalar_tensor_tensor(out=fsq_, in0=f, scalar=-0.5, in1=f,
                                               op0=ALU.mult, op1=ALU.mult).then_inc(fsq_done, 1)
                dve.wait_ge(fsq_done, count)
                nc.vector.tensor_reduce(g_, fsq_, AX_X, ALU.add).then_inc(g_done, 1)

            dve.wait_ge(w_loaded, 16)
            factor_sums(fsq[:, :, :], g_all[:, :], w_all[:, :, 0:E], 1)
            with dve.Fori(0, LAPS) as lap:
                for r in range(RING):
                    n = lap * RING + r
                    dve.wait_ge(loaded[r], (lap + 1) * 16)
                    dve.wait_ge(groups_used, n + 1)
                    square(sq[:, r % SLOTS, GROUP * B // 2:], x[:, r, GROUP * B // 2:], dve_squared)
            dve.wait_ge(par_loaded, 16)
            w_tail = par[:, C_TAIL:C_ALL].rearrange("p (c k) -> p c k", k=W)
            factor_sums(fsqt[:, :, :], gt[:, :], w_tail[:, :, 0:E], 2)
            nc.vector.tensor_tensor(bias[:, :], par[:, C_BLIN:C_BLIN + 1], par[:, C_B3:C_B3 + 1],
                                    ALU.add).then_inc(bias_done, 1)
            for t, c, n, rows in tail:
                dve.wait_ge(tail_loaded[t], 16)
                half = slice(c * B + n * HALF, (c + n) * B)
                square(sqt[0:rows, half], xt[0:rows, half], dve_squared)

            def relu(tiles, b, done):
                src, dst = tiles
                nc.vector.tensor_scalar(dst, src, b, 0.0, ALU.add, ALU.max).then_inc(done, 1)

            for q in range(0, TILES, 2):
                dve.wait_ge(h1_done, q + 1)
                relu(h1_of(q), b1, h1_relu[q])
            dve.wait_ge(sqs_copied, 1)
            nc.vector.tensor_copy(sqs_sb[:, HALF:B], sqs[:, HALF:B]).then_inc(sqs_copied, 1)
            for q in range(0, TILES, 2):
                dve.wait_ge(h2_done, q + 1)
                relu(h2_of(q), b2(q), h2_relu)
            dve.wait_ge(sig_done, 1)
            nc.vector.tensor_scalar(y[:, :], sig[:, :], 5.0, 0.5, ALU.mult, ALU.add).then_inc(y_done, 1)

        @block.tensor
        def _(pe):
            def add(acc, weights, data):
                return nc.tensor.matmul(acc, weights, data, start=False, stop=True, skip_group_check=True)

            pe.wait_ge(groups_used, SLOTS)
            for acc in (emb, sqs):
                for q in range(TILES):
                    nc.tensor.matmul(acc[QUAD * q:QUAD * (q + 1), :], zeros[:, 0:QUAD], zeros[:, :],
                                     start=True, stop=True)
            for acc in (sums, fin):
                nc.tensor.matmul(acc[:, 0:BLOCK], zeros[:, 0:P], zeros[:, 0:BLOCK], start=True, stop=True)

            def products(acc, weights, width, data, n, rows=P):
                pieces = TILES // n
                step = B // pieces
                for c in range(n):
                    for k in range(pieces):
                        q = QUAD * (c * pieces + k)
                        last = add(acc[q:q + width, k * step:(k + 1) * step],
                                   weights[0:rows, c * width:(c + 1) * width],
                                   data[0:rows, c * B + k * step:c * B + (k + 1) * step])
                return last

            with pe.Fori(0, LAPS) as lap:
                for r in range(RING):
                    n = lap * RING + r
                    pe.wait_ge(w_ready, n + 1)
                    pe.wait_ge(loaded[r], (lap + 1) * 16)
                    products(emb, w[:, r % SLOTS, :], W, x[:, r, :], GROUP)
                    pe.wait_ge(act_squared, n + 1)
                    pe.wait_ge(dve_squared, n + 1)
                    products(sqs, g[:, r % SLOTS, :], 1, sq[:, r % SLOTS, :], GROUP).then_inc(groups_used, 1)

            def tail_products(t):
                _, c, n, rows = tail[t]
                pe.wait_ge(tail_loaded[t], 16)
                return products(emb, par[:, C_TAIL + c * W:C_TAIL + (c + n) * W], W, xt[:, c * B:(c + n) * B], n, rows)

            def tail_square_products(t):
                _, c, n, rows = tail[t]
                pe.wait_ge(act_squared, GROUPS + t + 1)
                pe.wait_ge(dve_squared, GROUPS + t + 1)
                return products(sqs, gt[:, c:c + n], 1, sqt[:, c * B:(c + n) * B], n, rows)

            pe.wait_ge(par_loaded, 16)
            pe.wait_ge(g_done, 2)
            for t in range(len(TAIL) - 1):
                tail_products(t)
                if t < len(TAIL) - 2:
                    tail_square_products(t)
            tail_products(len(TAIL) - 1).then_inc(emb_done, 1)

            tail_square_products(len(TAIL) - 2)
            tail_square_products(len(TAIL) - 1).then_inc(sqs_done, 1)

            def row_product(acc, column, data):
                for q in range(TILES):
                    last = add(acc[QUAD * q:QUAD * q + 1, 0:BLOCK], par[:, column(q):column(q) + 1], data(q))
                return last

            def block_of(t):
                return lambda q: t[:, q * BLOCK:(q + 1) * BLOCK]

            for q in range(TILES):
                pe.wait_ge(emb_copied, q + 1)
                nc.tensor.matmul(h1_of(q)[0], par[:, C_W1:C_W1 + H1], emb_sb[:, q * BLOCK:(q + 1) * BLOCK],
                                 start=True, stop=True).then_inc(h1_done, 1)
            row_product(sums, lambda q: C_FAC, block_of(emb_sb)).then_inc(sums_done, 1)
            for q in range(TILES):
                pe.wait_ge(h1_relu[q], 1)
                nc.tensor.matmul(h2_of(q)[0], par[:, C_W2:C_W2 + H2], h1_of(q)[1],
                                 start=True, stop=True).then_inc(h2_done, 1)
            row_product(fin, lambda q: C_LIN, block_of(emb_sb))
            pe.wait_ge(sqs_copied, 2)
            row_product(fin, lambda q: C_SQ, block_of(sqs_sb))
            pe.wait_ge(s2_done, 1)
            row_product(fin, lambda q: C_HALF + q, lambda q: s2[:, :])
            pe.wait_ge(h2_relu, TILES)
            row_product(fin, lambda q: C_W3 + q // 2,
                        lambda q: h2_sb[:, q % 2 * BLOCK:(q % 2 + 1) * BLOCK]).then_inc(fin_done, 1)


def kernel(r_input_data, L0_rec_W_lin, L0_rec_b_lin, L0_rec_factors, L0_rec_W1, L0_rec_b1,
           L0_rec_W2, L0_rec_b2, L0_rec_W3, L0_rec_b3):
    import numpy as np
    import concourse.bacc as bacc
    from concourse.bass_utils import run_bass_kernel_spmd

    xt = np.asarray(r_input_data).T
    full = (CHUNKS - 1) * P
    x_loop = np.ascontiguousarray(
        xt[:LOOPED * P].reshape(GROUPS, GROUP, P, B).transpose(0, 2, 1, 3).reshape(GROUPS, P, GROUP * B))
    x_tail = np.ascontiguousarray(
        xt[LOOPED * P:full].reshape(TAIL_CHUNKS - 1, P, B).transpose(1, 0, 2).reshape(P, -1))
    x_end = np.ascontiguousarray(xt[full:])

    weights = np.zeros((CHUNKS * P, W), np.float32)
    weights[:D, 0:E] = np.asarray(L0_rec_factors)
    weights[:D, E] = np.asarray(L0_rec_W_lin)[0]
    weights = weights.reshape(CHUNKS, P, W).transpose(1, 0, 2)
    w_loop = np.ascontiguousarray(weights[:, :LOOPED])

    params = np.zeros((P, C_ALL), np.float32)
    for q in range(0, P, QUAD):
        params[q:q + E, C_W1:C_W1 + H1] = np.asarray(L0_rec_W1).T
        params[q + E, C_LIN] = 1
        params[q:q + E, C_FAC] = 1
        params[q, C_SQ] = 1
        params[q, C_HALF + q // QUAD] = 0.5
    params[:, C_W2:C_W2 + H2] = np.asarray(L0_rec_W2).T
    params[:, C_B1] = np.asarray(L0_rec_b1)
    for h in range(2):
        params[h * H2:(h + 1) * H2, C_W3 + h] = np.asarray(L0_rec_W3)[0]
        params[h * H2:(h + 1) * H2, C_B2] = np.asarray(L0_rec_b2)
    params[:, C_BLIN] = np.asarray(L0_rec_b_lin)[0]
    params[:, C_B3] = np.asarray(L0_rec_b3)[0]
    params[:, C_TAIL:] = weights[:, LOOPED:].reshape(P, -1)

    nc = bacc.Bacc("TRN2", target_bir_lowering=False, num_devices=1)
    arrays = {"w_loop": w_loop, "x_loop": x_loop, "x_tail": x_tail, "x_end": x_end, "params": params}
    args = [nc.dram_tensor(name, a.shape, F32, kind="ExternalInput").ap() for name, a in arrays.items()]
    args.append(nc.dram_tensor("out", (B,), F32, kind="ExternalOutput").ap())
    build(nc, *args)
    return run_bass_kernel_spmd(nc, [arrays], core_ids=[0]).results[0]["out"]
```

```python
from contextlib import ExitStack

import concourse.bass as bass
from concourse import mybir

F32 = mybir.dt.float32
BF16 = mybir.dt.bfloat16
ALU = mybir.AluOpType
ACT = mybir.ActivationFunctionType
AX_X = mybir.AxisListType.X

P = 128
B = 512
D = 12500
E = 16
H1, H2 = 128, 64
QUAD = 32
TILES = P // QUAD
HALF = B // 2
BLOCK = B // TILES

CHUNKS = -(-D // P)
LAST_ROWS = D - (CHUNKS - 1) * P
W = E + 1
GROUP = TILES
RING = 4
SLOTS = 2
LAPS = 5
GROUPS = LAPS * RING
LOOPED = GROUPS * GROUP
TAIL = (4, 4, 2, 2, 2, 2, 1, 1)
DIRECT = len(TAIL) - 4
TAIL_CHUNKS = CHUNKS - LOOPED
assert sum(TAIL) == TAIL_CHUNKS and TAIL[-1] == 1

C_W1 = 0
C_W2 = C_W1 + H1
C_W3 = C_W2 + H2
C_B1 = C_W3 + 2
C_B2 = C_B1 + 1
C_BIAS = C_B2 + 1
C_LIN = C_BIAS + 1
C_FAC = C_LIN + 1
C_SQ = C_FAC + 1
C_HALF = C_SQ + 1
C_TAIL = C_HALF + TILES
C_ALL = C_TAIL + TAIL_CHUNKS * W


def build(nc, w_loop, x_loop, x_tail, x_end, params, out):
    with ExitStack() as ctx:
        def sb(name, shape, dt=F32):
            return ctx.enter_context(nc.sbuf_tensor(name, shape, dt))

        def psum(name, shape):
            return ctx.enter_context(nc.psum_tensor(name, shape, F32))

        def sem(name):
            return ctx.enter_context(nc.semaphore(name))

        x = sb("x", [P, RING, GROUP * B])
        sq = sb("sq", [P, SLOTS, GROUP * B])
        xt = sb("xt", [P, TAIL_CHUNKS * B])
        sqt = sb("sqt", [P, TAIL_CHUNKS * B])
        w_all = sb("w_all", [P, LOOPED, W])
        fsq = sb("fsq", [P, LOOPED, E])
        g_all = sb("g_all", [P, LOOPED])
        fsqt = sb("fsqt", [P, TAIL_CHUNKS, E])
        gt = sb("gt", [P, TAIL_CHUNKS])
        w = sb("w", [P, SLOTS, GROUP * W])
        g = sb("g", [P, SLOTS, GROUP])
        par = sb("par", [P, C_ALL])
        zeros = sb("zeros", [P, B], BF16)
        warm = sb("warm", [P, 1])
        emb_sb = sb("emb_sb", [P, B])
        sqs_sb = sb("sqs_sb", [P, B])
        h1_sb = sb("h1_sb", [P, B])
        h2_sb = sb("h2_sb", [P, HALF])
        ones = sb("ones", [P, BLOCK])
        s2 = sb("s2", [P, BLOCK])
        sig = sb("sig", [P, BLOCK])
        y = sb("y", [P, BLOCK])

        emb = psum("emb", [P, B])
        sqs = psum("sqs", [P, B])
        h1 = [psum(f"h1_{q}", [P, B]) for q in range(TILES)]
        sums = psum("sums", [P, B])
        fin = psum("fin", [P, B])

        w_loaded = sem("w_loaded")
        loaded = [sem(f"loaded{r}") for r in range(RING)]
        tail_loaded = [sem(f"tail_loaded{t}") for t in range(len(TAIL))]
        par_loaded = sem("par_loaded")
        groups_used = sem("groups_used")
        w_ready = sem("w_ready")
        act_squared = sem("act_squared")
        dve_squared = sem("dve_squared")
        fsq_done = sem("fsq_done")
        g_done = sem("g_done")
        emb_done = sem("emb_done")
        sqs_done = sem("sqs_done")
        emb_copied = sem("emb_copied")
        sqs_copied = sem("sqs_copied")
        h1_done = sem("h1_done")
        h1_relu = [sem(f"h1_relu{q}") for q in range(TILES)]
        h2_done = sem("h2_done")
        h2_relu = sem("h2_relu")
        ones_set = sem("ones_set")
        sums_done = sem("sums_done")
        s2_done = sem("s2_done")
        fin_done = sem("fin_done")
        sig_done = sem("sig_done")
        y_done = sem("y_done")
        stored = sem("stored")

        tail = [(t, sum(TAIL[:t]), n, P if t < len(TAIL) - 1 else LAST_ROWS) for t, n in enumerate(TAIL)]

        def h1_of(q):
            return h1[q][:, 0:BLOCK], h1_sb[:, q * BLOCK:(q + 1) * BLOCK]

        def h2_of(q):
            rows = slice(q % 2 * H2, (q % 2 + 1) * H2)
            bank = (emb, h1[0])[q // 2]
            return bank[rows, 0:BLOCK], h2_sb[rows, q // 2 * BLOCK:(q // 2 + 1) * BLOCK]

        b1 = par[:, C_B1:C_B1 + 1]

        def b2(q):
            return par[q % 2 * H2:(q % 2 + 1) * H2, C_B2:C_B2 + 1]

        block = ctx.enter_context(nc.Block())

        @block.sync
        def _(sp):
            sp.dma_start(w_all[:, :, :], w_loop).then_inc(w_loaded, 16)
            for r in range(RING):
                sp.dma_start(x[:, r, :], x_loop[r]).then_inc(loaded[r], 16)
            sp.dma_start(par[:, :], params).then_inc(par_loaded, 16)
            with sp.Fori(1, LAPS) as lap:
                for r in range(RING):
                    sp.wait_ge(groups_used, SLOTS + (lap - 1) * RING + r + 1)
                    sp.dma_start(x[:, r, :], x_loop[bass.ds(lap * RING + r, 1)]).then_inc(loaded[r], 16)
            for t, c, n, rows in tail:
                src = x_end if t == len(TAIL) - 1 else x_tail[:, c * B:(c + n) * B]
                sp.dma_start(xt[0:rows, c * B:(c + n) * B], src).then_inc(tail_loaded[t], 16)
            sp.wait_ge(y_done, 1)
            sp.dma_start(out.rearrange("(q b) -> q b", b=BLOCK), y[::QUAD, :]).then_inc(stored, 16)
            sp.wait_ge(stored, 16)

        @block.gpsimd
        def _(pool):
            nc.gpsimd.memset(zeros[:, :], 0.0).then_inc(groups_used, SLOTS)
            nc.gpsimd.memset(ones[:, :], 1.0).then_inc(ones_set, 1)
            pool.wait_ge(w_loaded, 16)
            pool.wait_ge(g_done, 1)
            with pool.Fori(0, LAPS) as lap:
                for r in range(RING):
                    n = lap * RING + r
                    pool.wait_ge(groups_used, n + 1)
                    nc.gpsimd.tensor_copy(w[:, r % SLOTS, :].rearrange("p (c k) -> p c k", k=W),
                                          w_all[:, bass.ds(n * GROUP, GROUP), :])
                    nc.gpsimd.tensor_copy(g[:, r % SLOTS, :],
                                          g_all[:, bass.ds(n * GROUP, GROUP)]).then_inc(w_ready, 1)

        @block.scalar
        def _(act):
            nc.scalar.activation(warm[:, :], nc.const_aps.tensor(0.0, (P, 1), F32), ACT.Sigmoid)

            with act.Fori(0, LAPS) as lap:
                for r in range(RING):
                    n = lap * RING + r
                    act.wait_ge(loaded[r], (lap + 1) * 16)
                    act.wait_ge(groups_used, n + 1)
                    nc.scalar.activation(sq[:, r % SLOTS, 0:GROUP * B // 2], x[:, r, 0:GROUP * B // 2],
                                         ACT.Square).then_inc(act_squared, 1)
            for t, c, n, rows in tail:
                act.wait_ge(tail_loaded[t], 16)
                half = slice(c * B, c * B + n * HALF)
                nc.scalar.activation(sqt[0:rows, half], xt[0:rows, half], ACT.Square).then_inc(act_squared, 1)

            act.wait_ge(emb_done, 1)
            for q in range(TILES):
                cols = slice(q * BLOCK, (q + 1) * BLOCK)
                nc.scalar.copy(emb_sb[:, cols], emb[:, cols]).then_inc(emb_copied, 1)
            act.wait_ge(par_loaded, 16)
            for q in range(1, TILES, 2):
                act.wait_ge(h1_done, q + 1)
                src, dst = h1_of(q)
                nc.scalar.activation(dst, src, ACT.Relu, bias=b1).then_inc(h1_relu[q], 1)
            act.wait_ge(sums_done, 1)
            nc.scalar.activation(s2[:, :], sums[:, 0:BLOCK], ACT.Square).then_inc(s2_done, 1)
            for q in range(1, TILES, 2):
                act.wait_ge(h2_done, q + 1)
                src, dst = h2_of(q)
                nc.scalar.activation(dst, src, ACT.Relu, bias=b2(q)).then_inc(h2_relu, 1)
            act.wait_ge(fin_done, 1)
            nc.scalar.activation(sig[:, :], fin[:, 0:BLOCK], ACT.Sigmoid).then_inc(sig_done, 1)

        @block.vector
        def _(dve):
            def square(dst, src, done):
                nc.vector.tensor_tensor(dst, src, src, ALU.mult).then_inc(done, 1)

            def factor_sums(fsq_, g_, f, count):
                nc.vector.scalar_tensor_tensor(out=fsq_, in0=f, scalar=-0.5, in1=f,
                                               op0=ALU.mult, op1=ALU.mult).then_inc(fsq_done, 1)
                dve.wait_ge(fsq_done, count)
                nc.vector.tensor_reduce(g_, fsq_, AX_X, ALU.add).then_inc(g_done, 1)

            dve.wait_ge(w_loaded, 16)
            factor_sums(fsq[:, :, :], g_all[:, :], w_all[:, :, 0:E], 1)
            with dve.Fori(0, LAPS) as lap:
                for r in range(RING):
                    n = lap * RING + r
                    dve.wait_ge(loaded[r], (lap + 1) * 16)
                    dve.wait_ge(groups_used, n + 1)
                    square(sq[:, r % SLOTS, GROUP * B // 2:], x[:, r, GROUP * B // 2:], dve_squared)
            dve.wait_ge(par_loaded, 16)
            w_tail = par[:, C_TAIL:C_ALL].rearrange("p (c k) -> p c k", k=W)
            factor_sums(fsqt[:, :, :], gt[:, :], w_tail[:, :, 0:E], 2)
            for t, c, n, rows in tail:
                dve.wait_ge(tail_loaded[t], 16)
                half = slice(c * B + n * HALF, (c + n) * B)
                square(sqt[0:rows, half], xt[0:rows, half], dve_squared)
                if t == DIRECT:
                    dve.wait_ge(sqs_done, 1)
                    nc.vector.tensor_copy(sqs_sb[:, :], sqs[:, :]).then_inc(sqs_copied, 1)

            def relu(tiles, b, done):
                src, dst = tiles
                nc.vector.tensor_scalar(dst, src, b, 0.0, ALU.add, ALU.max).then_inc(done, 1)

            for q in range(0, TILES, 2):
                dve.wait_ge(h1_done, q + 1)
                relu(h1_of(q), b1, h1_relu[q])
            for q in range(0, TILES, 2):
                dve.wait_ge(h2_done, q + 1)
                relu(h2_of(q), b2(q), h2_relu)
            dve.wait_ge(sig_done, 1)
            nc.vector.tensor_scalar(y[:, :], sig[:, :], 5.0, 0.5, ALU.mult, ALU.add).then_inc(y_done, 1)

        @block.tensor
        def _(pe):
            def add(acc, weights, data):
                return nc.tensor.matmul(acc, weights, data, start=False, stop=True, skip_group_check=True)

            pe.wait_ge(groups_used, SLOTS)
            for acc in (emb, sqs):
                for q in range(TILES):
                    nc.tensor.matmul(acc[QUAD * q:QUAD * (q + 1), :], zeros[:, 0:QUAD], zeros[:, :],
                                     start=True, stop=True)
            for acc in (sums, fin):
                nc.tensor.matmul(acc[:, 0:BLOCK], zeros[:, 0:P], zeros[:, 0:BLOCK], start=True, stop=True)

            def products(acc, weights, width, data, n, rows=P):
                pieces = TILES // n
                step = B // pieces
                for c in range(n):
                    for k in range(pieces):
                        q = QUAD * (c * pieces + k)
                        last = add(acc[q:q + width, k * step:(k + 1) * step],
                                   weights[0:rows, c * width:(c + 1) * width],
                                   data[0:rows, c * B + k * step:c * B + (k + 1) * step])
                return last

            with pe.Fori(0, LAPS) as lap:
                for r in range(RING):
                    n = lap * RING + r
                    pe.wait_ge(w_ready, n + 1)
                    pe.wait_ge(loaded[r], (lap + 1) * 16)
                    products(emb, w[:, r % SLOTS, :], W, x[:, r, :], GROUP)
                    pe.wait_ge(act_squared, n + 1)
                    pe.wait_ge(dve_squared, n + 1)
                    products(sqs, g[:, r % SLOTS, :], 1, sq[:, r % SLOTS, :], GROUP).then_inc(groups_used, 1)

            def row_product(acc, column, data):
                for q in range(TILES):
                    last = add(acc[QUAD * q:QUAD * q + 1, 0:BLOCK], column(q), data(q))
                return last

            def par_column(c):
                return par[:, c:c + 1]

            def block_of(t):
                return lambda q: t[:, q * BLOCK:(q + 1) * BLOCK]

            def tail_products(t):
                _, c, n, rows = tail[t]
                pe.wait_ge(tail_loaded[t], 16)
                return products(emb, par[:, C_TAIL + c * W:C_TAIL + (c + n) * W], W, xt[:, c * B:(c + n) * B], n, rows)

            def tail_square_products(t):
                _, c, n, rows = tail[t]
                pe.wait_ge(act_squared, GROUPS + t + 1)
                pe.wait_ge(dve_squared, GROUPS + t + 1)
                if t < DIRECT:
                    return products(sqs, gt[:, c:c + n], 1, sqt[:, c * B:(c + n) * B], n, rows)
                for k in range(c, c + n):
                    last = row_product(fin, lambda q: gt[0:rows, k:k + 1],
                                       lambda q: sqt[0:rows, k * B + q * BLOCK:k * B + (q + 1) * BLOCK])
                return last

            pe.wait_ge(par_loaded, 16)
            pe.wait_ge(g_done, 2)
            pe.wait_ge(ones_set, 1)
            row_product(fin, lambda q: par_column(C_BIAS), lambda q: ones[:, :])
            for t in range(DIRECT):
                tail_products(t)
                last = tail_square_products(t)
            last.then_inc(sqs_done, 1)
            for t in range(DIRECT, len(TAIL) - 3):
                tail_products(t)
                tail_square_products(t)
            pe.wait_ge(sqs_copied, 1)
            row_product(fin, lambda q: par_column(C_SQ), block_of(sqs_sb))
            tail_products(len(TAIL) - 3)
            tail_products(len(TAIL) - 2)
            tail_square_products(len(TAIL) - 3)
            tail_products(len(TAIL) - 1).then_inc(emb_done, 1)
            tail_square_products(len(TAIL) - 2)
            tail_square_products(len(TAIL) - 1)

            for q in range(TILES):
                pe.wait_ge(emb_copied, q + 1)
                nc.tensor.matmul(h1_of(q)[0], par[:, C_W1:C_W1 + H1], emb_sb[:, q * BLOCK:(q + 1) * BLOCK],
                                 start=True, stop=True).then_inc(h1_done, 1)
            row_product(sums, lambda q: par_column(C_FAC), block_of(emb_sb)).then_inc(sums_done, 1)
            for q in range(TILES):
                pe.wait_ge(h1_relu[q], 1)
                nc.tensor.matmul(h2_of(q)[0], par[:, C_W2:C_W2 + H2], h1_of(q)[1],
                                 start=True, stop=True).then_inc(h2_done, 1)
            row_product(fin, lambda q: par_column(C_LIN), block_of(emb_sb))
            pe.wait_ge(s2_done, 1)
            row_product(fin, lambda q: par_column(C_HALF + q), lambda q: s2[:, :])
            pe.wait_ge(h2_relu, TILES)
            row_product(fin, lambda q: par_column(C_W3 + q % 2),
                        lambda q: h2_sb[:, q // 2 * BLOCK:(q // 2 + 1) * BLOCK]).then_inc(fin_done, 1)


def kernel(r_input_data, L0_rec_W_lin, L0_rec_b_lin, L0_rec_factors, L0_rec_W1, L0_rec_b1,
           L0_rec_W2, L0_rec_b2, L0_rec_W3, L0_rec_b3):
    import numpy as np
    import concourse.bacc as bacc
    from concourse.bass_utils import run_bass_kernel_spmd

    xt = np.asarray(r_input_data).T
    full = (CHUNKS - 1) * P
    x_loop = np.ascontiguousarray(
        xt[:LOOPED * P].reshape(GROUPS, GROUP, P, B).transpose(0, 2, 1, 3).reshape(GROUPS, P, GROUP * B))
    x_tail = np.ascontiguousarray(
        xt[LOOPED * P:full].reshape(TAIL_CHUNKS - 1, P, B).transpose(1, 0, 2).reshape(P, -1))
    x_end = np.ascontiguousarray(xt[full:])

    weights = np.zeros((CHUNKS * P, W), np.float32)
    weights[:D, 0:E] = np.asarray(L0_rec_factors)
    weights[:D, E] = np.asarray(L0_rec_W_lin)[0]
    weights = weights.reshape(CHUNKS, P, W).transpose(1, 0, 2)
    w_loop = np.ascontiguousarray(weights[:, :LOOPED])

    params = np.zeros((P, C_ALL), np.float32)
    for q in range(0, P, QUAD):
        params[q:q + E, C_W1:C_W1 + H1] = np.asarray(L0_rec_W1).T
        params[q + E, C_LIN] = 1
        params[q:q + E, C_FAC] = 1
        params[q, C_SQ] = 1
        params[q, C_HALF + q // QUAD] = 0.5
    params[:, C_W2:C_W2 + H2] = np.asarray(L0_rec_W2).T
    params[:, C_B1] = np.asarray(L0_rec_b1)
    for h in range(2):
        params[h * H2:(h + 1) * H2, C_W3 + h] = np.asarray(L0_rec_W3)[0]
        params[h * H2:(h + 1) * H2, C_B2] = np.asarray(L0_rec_b2)
    params[0, C_BIAS] = np.asarray(L0_rec_b_lin)[0]
    params[1, C_BIAS] = np.asarray(L0_rec_b3)[0]
    params[:, C_TAIL:] = weights[:, LOOPED:].reshape(P, -1)

    nc = bacc.Bacc("TRN2", target_bir_lowering=False, num_devices=1)
    arrays = {"w_loop": w_loop, "x_loop": x_loop, "x_tail": x_tail, "x_end": x_end, "params": params}
    args = [nc.dram_tensor(name, a.shape, F32, kind="ExternalInput").ap() for name, a in arrays.items()]
    args.append(nc.dram_tensor("out", (B,), F32, kind="ExternalOutput").ap())
    build(nc, *args)
    return run_bass_kernel_spmd(nc, [arrays], core_ids=[0]).results[0]["out"]
```
